# Optimizing a Trainium2 kernel written in Bass

```python
import numpy as np
import jax
import jax.numpy as jnp

def _softmax(x, axis=-1):
    return jax.nn.softmax(x, axis=axis)
def _gelu(x):
    return jax.nn.gelu(x, approximate=True)
def _silu(x):
    return jax.nn.silu(x)
def _sigmoid(x):
    return jax.nn.sigmoid(x)
def _layernorm(x, axis=-1, eps=1e-5):
    m = jnp.mean(x, axis=axis, keepdims=True)
    v = jnp.var(x, axis=axis, keepdims=True)
    return (x - m) / jnp.sqrt(v + eps)
def _scatter_add(tgt, idx, src, axis=0):
    return tgt.at[idx].add(src)
def _segment_sum(src, seg, n):
    return jax.ops.segment_sum(src, seg, n)

kernel_name = 'mk_conv_preact_d1_conv_nhwc256_78d74f'

def setup_inputs(seed: int = 0):
    np.random.seed(seed)
    _w = jnp.asarray
    def _rec_inputs():
        import jax
        import jax.numpy as jnp
        _gk = jax.random.key(seed)
        x = -0.0003929 + 0.9999 * jax.random.normal(jax.random.fold_in(_gk, 1), (1, 256, 256, 256), jnp.float32)
        return x
    x = _rec_inputs()
    def _L0_conv_setup():
        import jax, jax.numpy as jnp
        import numpy as np
        EPS = 1e-05

        def _to_heads(x, B, s, i, h, d):
            return jnp.transpose(x.reshape(B, s, i, h, d), (0, 2, 3, 1, 4))
        key = jax.random.key(seed)
        ks = jax.random.split(key, 8)
        B, s, i, c = (1, 256, 256, 256)
        h, d = (8, 32)
        m = jax.random.normal(ks[0], (B, s, i, c), dtype=jnp.float32)
        msa_mask = jnp.ones((B, s, i), dtype=jnp.float32)
        sc = 1.0 / np.sqrt(c)
        return {'m': m, 'msa_mask': msa_mask, 'ln_w': jnp.ones((c,), jnp.float32), 'ln_b': jnp.zeros((c,), jnp.float32), 'wq': jax.random.normal(ks[1], (h * d, c), jnp.float32) * sc, 'wk': jax.random.normal(ks[2], (h * d, c), jnp.float32) * sc, 'wv': jax.random.normal(ks[3], (h * d, c), jnp.float32) * sc, 'wg': jax.random.normal(ks[4], (h * d, c), jnp.float32) * sc, 'bg': jnp.zeros((h * d,), jnp.float32), 'wo': jax.random.normal(ks[5], (c, h * d), jnp.float32) * sc, 'bo': jnp.zeros((c,), jnp.float32)}
    _L0_conv_all = _L0_conv_setup()
    _L0_conv_in = {k: v for k, v in _L0_conv_all.items() if k in ('msa_mask', 'ln_w', 'ln_b', 'wq', 'wk', 'wv', 'wg', 'bg', 'wo', 'bo', )}
    del _L0_conv_all

    return {
        "x": x,
        "L0_conv_msa_mask": _L0_conv_in["msa_mask"],
        "L0_conv_ln_w": _L0_conv_in["ln_w"],
        "L0_conv_ln_b": _L0_conv_in["ln_b"],
        "L0_conv_wq": _L0_conv_in["wq"],
        "L0_conv_wk": _L0_conv_in["wk"],
        "L0_conv_wv": _L0_conv_in["wv"],
        "L0_conv_wg": _L0_conv_in["wg"],
        "L0_conv_bg": _L0_conv_in["bg"],
        "L0_conv_wo": _L0_conv_in["wo"],
        "L0_conv_bo": _L0_conv_in["bo"],
    }

def reference(x, L0_conv_msa_mask, L0_conv_ln_w, L0_conv_ln_b, L0_conv_wq, L0_conv_wk, L0_conv_wv, L0_conv_wg, L0_conv_bg, L0_conv_wo, L0_conv_bo):
    import jax
    import jax.numpy as jnp
    def _L0_conv_ref(m, msa_mask, ln_w, ln_b, wq, wk, wv, wg, bg, wo, bo):
        import jax, jax.numpy as jnp
        import numpy as np
        EPS = 1e-05

        def _to_heads(x, B, s, i, h, d):
            return jnp.transpose(x.reshape(B, s, i, h, d), (0, 2, 3, 1, 4))
        B, s, i, c = m.shape
        hd = wq.shape[0]
        d = 32
        h = hd // d
        mu = jnp.mean(m, axis=-1, keepdims=True)
        var = jnp.mean(jnp.square(m - mu), axis=-1, keepdims=True)
        m_norm = (m - mu) * jax.lax.rsqrt(var + EPS) * ln_w + ln_b
        q = _to_heads(m_norm @ wq.T, B, s, i, h, d)
        k = _to_heads(m_norm @ wk.T, B, s, i, h, d)
        v = _to_heads(m_norm @ wv.T, B, s, i, h, d)
        gate = jax.nn.sigmoid(_to_heads(m_norm @ wg.T + bg, B, s, i, h, d))
        mk = jnp.transpose(msa_mask, (0, 2, 1)) > 0
        mv = mk.astype(q.dtype)[:, :, None, :, None]
        q = q * mv
        k = k * mv
        v = v * mv
        gate = gate * mv
        logits = jnp.einsum('bihqd,bihkd->bihqk', q, k) / jnp.sqrt(jnp.asarray(d, q.dtype))
        pair_mask = (mk[:, :, None, :] & mk[:, :, :, None])[:, :, None, :, :]
        logits = jnp.where(pair_mask, logits, jnp.asarray(-1000000000.0, q.dtype))
        attn = jax.nn.softmax(logits, axis=-1)
        o = jnp.einsum('bihqk,bihkd->bihqd', attn, v)
        o = o * gate * mv
        o = jnp.transpose(o, (0, 1, 3, 2, 4)).reshape(B, i, s, h * d)
        o = o @ wo.T + bo
        return jnp.transpose(o, (0, 2, 1, 3))

    def _gn(v, G=32, eps=1e-5):
        B_, H_, W_, C_ = v.shape
        g = v.reshape(B_, H_, W_, G, C_ // G)
        m = jnp.mean(g, axis=(1, 2, 4), keepdims=True)
        s = jnp.var(g, axis=(1, 2, 4), keepdims=True)
        return ((g - m) / jnp.sqrt(s + eps)).reshape(v.shape)

    def _ln_c(v, eps=1e-6):
        m = jnp.mean(v, axis=-1, keepdims=True)
        s = jnp.var(v, axis=-1, keepdims=True)
        return (v - m) / jnp.sqrt(s + eps)

    def _ln_t(v, eps=1e-5):
        m = jnp.mean(v, axis=-1, keepdims=True)
        s = jnp.var(v, axis=-1, keepdims=True)
        return (v - m) / jnp.sqrt(s + eps)

    def _to_tokens(v):
        B_, H_, W_, C_ = v.shape
        return v.reshape(B_, H_ * W_, C_)
    def _from_tokens(t, like):
        return t.reshape(like.shape)

    x = x + _L0_conv_ref(_gn(x), L0_conv_msa_mask, L0_conv_ln_w, L0_conv_ln_b, L0_conv_wq, L0_conv_wk, L0_conv_wv, L0_conv_wg, L0_conv_bg, L0_conv_wo, L0_conv_bo)
    return x


_drawn_inputs = setup_inputs


def setup_inputs(seed=0):
    import zlib

    import numpy as np

    out = dict(_drawn_inputs(seed))
    spreads = {'L0_conv_ln_w': (1.0, 0.2),
     'L0_conv_ln_b': (0.0, 0.1),
     'L0_conv_bg': (0.0, 2.0),
     'L0_conv_bo': (0.0, 0.1)}
    factors = {}
    for name, (base, spread) in spreads.items():
        noise = np.random.default_rng([zlib.crc32(name.encode()), seed]).standard_normal(out[name].shape)
        drawn = base * np.exp(spread * noise) if base else spread * noise
        out[name] = jnp.asarray(drawn.astype(out[name].dtype))
    for name, factor in factors.items():
        out[name] = (out[name] * factor).astype(out[name].dtype)
    return out
```

```python
import concourse.bass as bass
from concourse import mybir
import numpy as np
from contextlib import ExitStack

F32 = mybir.dt.float32
F32R = mybir.dt.float32r
F16 = mybir.dt.float16
BF16 = mybir.dt.bfloat16
ALU = mybir.AluOpType
ACT = mybir.ActivationFunctionType
X = mybir.AxisListType.X

P = 128
HEAD_DIM = 32
GROUPS = 32
GN_EPS = 1e-5
LN_EPS = 1e-5
MASKED = -1e9
TINY = 1e-30
STAT_TOKENS = 32

JOBS = [
    (0, "A", "zt", 0, 1), (0, "PV", "o", -1, 0), (0, "B", "g", 0, 0),
    (1, "A", "zt", 1, 1), (1, "PV", "o", 0, 0), (1, "B", "g", 1, 0),
    (2, "A", "ot", 1, -1), (2, "PV", "o", 1, 0), (2, "B", "q", 0, 1),
    (3, "PV", "o", 2, 0), (3, "B", "k", 0, 1),
    (4, "A", "out", 1, -1), (4, "PV", "o", 3, 0), (4, "B", "q", 1, 1),
    (5, "A", "ot", 0, 0), (5, "PV", "o", 4, 0), (5, "B", "k", 1, 1),
    (6, "PV", "o", 5, 0), (6, "B", "v", 0, 1),
    (7, "A", "out", 0, 0), (7, "PV", "o", 6, 0), (7, "B", "v", 1, 1),
]
EXPS_FIRST = (0, 1, 5)
PROLOGUE = [("zt", 0), ("zt", 1), ("q", 0), ("k", 0), ("q", 1), ("k", 1), ("v", 0), ("v", 1)]
KINDS = ("zt", "q", "k", "v", "g", "o", "ot", "out")
PER_PAIR = {k: 8 if k == "o" else 2 for k in KINDS}
BANK = {(kind, number % 8 if kind == "o" else number): n % 2 for n, (_, _, kind, number, _) in enumerate(JOBS)}


def build_msa(nc, x, mask, ln_w, ln_b, wq, wk, wv, wg, bg, wo, bo, out):
    _, S, I, C = x.shape
    HD = wq.shape[0]
    NQ = S // P
    NC = C // P
    NM = HD // P
    NH = HD // HEAD_DIM
    PAIRS = I // 2
    CHUNKS = 8
    STAT_TILES = S * I // (P * STAT_TOKENS)
    GC = C // GROUPS
    MW = min(P, I)
    MT = I // MW
    assert (NQ, NC, NM, NH) == (2, 2, 2, 8) and PAIRS % 2 == 0 and PAIRS >= 4
    SCALE = float(HEAD_DIM) ** -0.5

    x_stat = x.rearrange("b (j r) i c -> (b j) (r i c)", j=STAT_TILES).rearrange("j (p n) -> j p n", p=P)
    x_cols = x.rearrange("b (q p) i c -> p (b q) i c", p=P)
    out_cols = out.rearrange("b (q p) i c -> p (b q) i c", p=P)

    ctx = ExitStack()
    with ctx:
        def sb(name, shape, dt=F32):
            return ctx.enter_context(nc.sbuf_tensor(name, shape, dt))

        def sem(name):
            return ctx.enter_context(nc.semaphore(name))

        ident = sb("ident", [P, P])
        mean_mat = sb("mean_mat", [P, P])
        minus_half = sb("minus_half", [P, 4])
        ln_eps = sb("ln_eps", [P, 4])
        half_col = sb("half_col", [P, 1])
        wait_carrier = sb("wait_carrier", [P, 1])
        lnw_row = sb("lnw_row", [P, C])
        lnb_row = sb("lnb_row", [P, C])
        bo_row = sb("bo_row", [P, C])
        bg_col = sb("bg_col", [P, NM])
        keep = sb("keep", [P, NQ, I])
        mask_bias = sb("mask_bias", [P, NQ, I])
        mask_bias_t = sb("mask_bias_t", [P, MT, S], BF16)
        column_hot = sb("column_hot", [P, MT * I], BF16)
        kept_min = sb("kept_min", [P, 1])
        kept_row = sb("kept_row", [1, P])
        masked_flag = sb("masked_flag", [1, 1], mybir.dt.int32)
        w_nat = {n: sb(f"w_nat_{n}", [P, NM, C]) for n in "qkvgo"}
        w_hi = {n: sb(f"w_hi_{n}", [P, NC, HD], F32R) for n in "qkvgo"}
        w_lo = {n: sb(f"w_lo_{n}", [P, NC, HD], F32R) for n in "qkvgo"}
        w_tmp = sb("w_tmp", [P, NM, C])
        bias = {n: sb(f"bias_{n}", [P, NM]) for n in "qkvg"}
        v_scale = sb("v_scale", [P, NM])
        v_rscale = sb("v_rscale", [P, NM])
        TILE = STAT_TOKENS * C
        xs_flat = sb("xs", [P, 2 * TILE])
        xs = xs_flat[:, :].rearrange("p (b n) -> p b n", b=2)
        gn_stats = sb("gn_stats", [P, GROUPS, STAT_TILES, 6])
        gn_part = sb("gn_part", [P, GROUPS, 2])
        gn_mean = sb("gn_mean", [P, GROUPS])
        gn_dev = sb("gn_dev", [P, GROUPS])
        gn_var = sb("gn_var", [P, GROUPS])
        gn_rstd = sb("gn_rstd", [P, GROUPS])
        gn_shift = sb("gn_shift", [P, GROUPS])
        gn_scale_row = sb("gn_scale_row", [P, C])
        gn_shift_row = sb("gn_shift_row", [P, C])
        placed = [0]

        def over_xs(*shape):
            n = int(np.prod(shape))
            placed[0] += n
            dims = {f"d{i}": d for i, d in enumerate(shape)}
            names = " ".join(dims)
            return xs_flat[:, placed[0] - n:placed[0]].rearrange(f"p ({names}) -> p {names}", **dims)

        xt = sb("xt", [P, 2, NQ, 2, C])
        xb = over_xs(2, NQ, 2, C)
        xn = sb("xn", [P, NQ * 2, C])
        z = over_xs(NQ, 2, C)
        row_stats = sb("row_stats", [P, NQ * 2, 6])
        row_mv = sb("row_mv", [P, NQ * 2, 2])
        row_rstd = sb("row_rstd", [P, NQ * 2])
        zt = [[sb(f"zt{part}{b}", [P, NC, 2 * S], F32R) for part in ("hi", "lo")] for b in range(2)]
        qt = [[sb(f"q{part}{b}", [P, NM, 2 * S], F32R) for part in ("hi", "lo")] for b in range(2)]
        kt = [[sb(f"k{part}{b}", [P, NM, 2 * S], F32R) for part in ("hi", "lo")] for b in range(2)]
        vt = [[sb(f"v{part}{b}", [P, 2, NQ, NH, HEAD_DIM + 1], F16) for part in ("hi", "lo")] for b in range(2)]
        gt = over_xs(2, NM, 2 * S)
        neg_max = sb("neg_max", [P, 2, 4])
        row_rsum = sb("row_rsum", [P, 4])
        probs = over_xs(2, 4, S)
        pt = [sb("pt_hi", [P, 2, 4, P], F16), sb("pt_lo", [P, 2, 4, P], F16)]
        o_rows = over_xs(2, NQ, HD)
        og = over_xs(NM, S)
        ogt = [sb("og_hi", [P, NM, S], F32R), sb("og_lo", [P, NM, S], F32R)]

        psum = ctx.enter_context(nc.psum_tensor("psum", [P, 8, 512], F32))
        logits = [psum[:, 2 * b:2 * b + 2, :] for b in range(2)]
        pt_psum = psum[:, 4:6, :]
        job_psum = [psum[:, 6, :], psum[:, 7, :]]

        s_const = sem("s_const")
        s_consts_loaded = sem("s_consts_loaded")
        s_weights_loaded = sem("s_weights_loaded")
        s_stat_x = [sem(f"s_stat_x{b}") for b in range(2)]
        s_stat_used = sem("s_stat_used")
        s_dve = sem("s_dve")
        s_pool = sem("s_pool")
        s_w_folded = sem("s_w_folded")
        s_w_transposed = sem("s_w_transposed")
        s_w_split = sem("s_w_split")
        s_gn_partial = sem("s_gn_partial")
        s_gn_summed = sem("s_gn_summed")
        s_gn_rows = sem("s_gn_rows")
        s_setup = sem("s_setup")
        s_gn_var = sem("s_gn_var")
        s_x = [sem(f"s_x{b}") for b in range(2)]
        s_stored = [sem(f"s_stored{b}") for b in range(2)]
        s_xb = sem("s_xb")
        s_affine = sem("s_affine")
        s_row_stats_own = sem("s_row_stats_own")
        s_row_stats = sem("s_row_stats")
        s_row_rstd = sem("s_row_rstd")
        s_z = sem("s_z")
        s_filled = {k: sem(f"s_{k}_filled") for k in KINDS}
        s_hi = {k: sem(f"s_{k}_hi") for k in ("zt", "q", "k", "v", "ot")}
        s_drained = {k: sem(f"s_{k}_drained") for k in KINDS}
        s_og_lo = sem("s_og_lo")
        s_gate = sem("s_gate")
        s_logits = sem("s_logits")
        s_max = sem("s_max")
        s_exp = sem("s_exp")
        s_pt = sem("s_pt")
        s_pt_hi = sem("s_pt_hi")
        s_pt_lo = sem("s_pt_lo")
        s_rsum = sem("s_rsum")

        block = ctx.enter_context(nc.Block())

        def bank_of(kind, number):
            return job_psum[BANK[kind, number]]

        def count(kind, number, pair):
            return pair * PER_PAIR[kind] + (number + 1)

        def over_pairs(eng, body):
            body(0, 0, 0, True, False)
            with eng.Fori(0, PAIRS // 2 - 1) as u:
                body(2 * u + 1, u, 1, False, False)
                body(2 * u + 2, u + 1, 0, False, False)
            body(PAIRS - 1, PAIRS // 2 - 1, 1, False, True)

        def jobs(slot, place, first, last):
            for s, pl, kind, number, dp in JOBS:
                if s == slot and pl == place and not (last and dp == 1):
                    if not (first and (dp == -1 or number == -1)):
                        yield kind, number, dp

        @block.sync
        def _(sp):
            for n, w in (("q", wq), ("k", wk), ("v", wv), ("g", wg), ("o", wo)):
                sp.dma_start(w_nat[n][:, :, :], w.rearrange("(m p) c -> p m c", p=P)).then_inc(s_weights_loaded, 16)
            sp.dma_start(lnw_row[:, :], ln_w.partition_broadcast(P)).then_inc(s_consts_loaded, 16)
            sp.dma_start(lnb_row[:, :], ln_b.partition_broadcast(P)).then_inc(s_consts_loaded, 16)
            sp.dma_start(bo_row[:, :], bo.partition_broadcast(P)).then_inc(s_consts_loaded, 16)
            sp.dma_start(bg_col[:, :], bg.rearrange("(m p) -> p m", p=P),
                         allow_slow_non_contiguous=True).then_inc(s_consts_loaded, 16)
            sp.dma_start(mask_bias[:, :, :], mask.rearrange("b (q p) i -> p (b q) i", p=P)).then_inc(s_consts_loaded, 16)
            for b in range(2):
                sp.dma_start(xs[:, b, :], x_stat[b]).then_inc(s_stat_x[b], 16)
            with (sp.Fori(1, STAT_TILES // 2) if STAT_TILES > 2 else ExitStack()) as j:
                for b in range(2 if STAT_TILES > 2 else 0):
                    sp.wait_ge(s_stat_used, 2 * j + (b - 1))
                    sp.dma_start(xs[:, b, :], x_stat[bass.ds(2 * j + b, 1)].rearrange("a p n -> (a p) n"))\
                      .then_inc(s_stat_x[b], 16)
            for b in range(2):
                sp.dma_start(xt[:, b], x_cols[:, :, 2 * b:2 * b + 2, :]).then_inc(s_x[b], 16)

            def body(pair, half, par, first, last):
                if not last:
                    if not (isinstance(pair, int) and pair + 2 >= PAIRS):
                        sp.wait_ge(s_xb, pair + 1)
                        sp.dma_start(xt[:, par], x_cols[:, :, bass.ds(2 * pair + 4, 2), :]).then_inc(s_x[par], 16)
                if not first:
                    sp.wait_ge(s_drained["out"], 2 * pair)
                    sp.dma_start(out_cols[:, :, bass.ds(2 * pair - 2, 2), :], xb[:, 1 - par])\
                      .then_inc(s_stored[1 - par], 16)

            body(0, 0, 0, True, False)
            with sp.Fori(0, PAIRS // 2 - 2) as u:
                body(2 * u + 1, u, 1, False, False)
                body(2 * u + 2, u + 1, 0, False, False)
            body(PAIRS - 3, PAIRS // 2 - 2, 1, False, False)
            body(PAIRS - 2, PAIRS // 2 - 1, 0, False, False)
            body(PAIRS - 1, PAIRS // 2 - 1, 1, False, True)
            sp.wait_ge(s_drained["out"], 2 * PAIRS)
            sp.dma_start(out_cols[:, :, 2 * PAIRS - 2:2 * PAIRS, :], xb[:, 1]).then_inc(s_stored[1], 16)
            sp.wait_ge(s_stored[0], 16 * (PAIRS // 2))
            sp.wait_ge(s_stored[1], 16 * (PAIRS // 2))

        @block.gpsimd
        def _(pool):
            chain = [0]

            def link(ins):
                chain[0] += 1
                ins.then_inc(s_pool, 1)
                pool.wait_ge(s_pool, chain[0])

            link(nc.gpsimd.memset(ident[:, :], 0.0))
            link(nc.gpsimd.affine_select(out=ident[:, :], in_=ident[:, :], compare_op=ALU.not_equal, fill=1.0,
                                         base=0, pattern=[[-1, P]], channel_multiplier=1))
            nc.gpsimd.memset(mean_mat[:, :], 1.0 / P)
            nc.gpsimd.memset(ln_eps[:, :], LN_EPS)
            nc.gpsimd.memset(half_col[:, :], 0.5)
            link(nc.gpsimd.memset(column_hot[:, :], 0.0))
            for a in range(MT):
                at = a * I + a * MW
                link(nc.gpsimd.affine_select(out=column_hot[:, at:at + MW], in_=column_hot[:, at:at + MW],
                                             compare_op=ALU.not_equal, fill=1.0, base=0, pattern=[[-1, MW]],
                                             channel_multiplier=1))
            for b in range(2):
                nc.gpsimd.memset(vt[b][0][:, :, :, :, HEAD_DIM:HEAD_DIM + 1], 1.0)
            nc.gpsimd.memset(minus_half[:, :], -0.5).then_inc(s_const, 1)

            pool.wait_ge(s_gn_var, 1)
            link(nc.gpsimd.tensor_scalar(gn_var[:, :], gn_var[:, :], GN_EPS, None, ALU.add))
            nc.gpsimd.tensor_tensor(gn_rstd[:, :], gn_var[:, :],
                                    minus_half[:, 0:1].to_broadcast([P, GROUPS]), ALU.pow).then_inc(s_setup, 1)
            pool.wait_ge(s_gn_rows, 1)

            def affine(pair, half, par):
                pool.wait_ge(s_x[par], 16 * (half + 1))
                if not (isinstance(pair, int) and pair == 0):
                    pool.wait_ge(s_z, 2 * pair)
                rows = gn_scale_row[:, :].unsqueeze(1).to_broadcast([P, NQ * 2, C])
                shift = gn_shift_row[:, :].unsqueeze(1).to_broadcast([P, NQ * 2, C])
                src = xt[:, par].rearrange("p q i c -> p (q i) c")
                nc.gpsimd.tensor_tensor(xn[:, :, :], src, rows, ALU.mult).then_inc(s_affine, 1)
                pool.wait_ge(s_affine, 2 * pair + 1)
                nc.gpsimd.tensor_tensor(xn[:, :, :], xn[:, :, :], shift, ALU.add).then_inc(s_affine, 1)

            def make_z(pair):
                pool.wait_ge(s_row_stats, pair + 1)
                nc.gpsimd.tensor_tensor(row_rstd[:, :], row_mv[:, :, 1], ln_eps[:, :], ALU.add).then_inc(s_row_rstd, 1)
                pool.wait_ge(s_row_rstd, 2 * pair + 1)
                nc.gpsimd.tensor_tensor(row_rstd[:, :], row_rstd[:, :], minus_half[:, :], ALU.pow)\
                         .then_inc(s_row_rstd, 1)
                pool.wait_ge(s_row_rstd, 2 * pair + 2)
                if not (isinstance(pair, int) and pair == 0):
                    pool.wait_ge(s_filled["zt"], 2 * pair)
                rows = [P, NQ * 2, C]
                z_rows = z.rearrange("p q i c -> p (q i) c")
                nc.gpsimd.tensor_tensor(z_rows, xn[:, :, :], row_mv[:, :, 0:1].to_broadcast(rows), ALU.subtract)\
                         .then_inc(s_z, 1)
                pool.wait_ge(s_z, 2 * pair + 1)
                nc.gpsimd.tensor_tensor(z_rows, z_rows, row_rstd[:, :].unsqueeze(2).to_broadcast(rows), ALU.mult)\
                         .then_inc(s_z, 1)

            def add_bo(pair, half, par):
                if not (isinstance(pair, int) and pair < 2):
                    pool.wait_ge(s_stored[par], 16 * half)
                bo_rows = bo_row[:, :].unsqueeze(1).to_broadcast([P, NQ * 2, C])
                nc.gpsimd.tensor_tensor(xb[:, par].rearrange("p q i c -> p (q i) c"),
                                        xt[:, par].rearrange("p q i c -> p (q i) c"), bo_rows, ALU.add)\
                         .then_inc(s_xb, 1)

            def og_lo(number, pair):
                pool.wait_ge(s_hi["ot"], count("ot", number, pair))
                nc.gpsimd.tensor_tensor(ogt[1][:, :, :], og[:, :, :], ogt[0][:, :, :].bitcast(F32), ALU.subtract)\
                         .then_inc(s_og_lo, 1)

            def gate(number, pair, par):
                pool.wait_ge(s_drained["g"], count("g", number, pair))
                nc.gpsimd.tensor_tensor(gt[:, par, number, :], gt[:, par, number, :],
                                        half_col[:, 0:1].to_broadcast([P, 2 * S]), ALU.mult).then_inc(s_gate, 1)
                pool.wait_ge(s_gate, 4 * pair + 2 * number + 1)
                nc.gpsimd.tensor_tensor(gt[:, par, number, :], gt[:, par, number, :],
                                        half_col[:, 0:1].to_broadcast([P, 2 * S]), ALU.add).then_inc(s_gate, 1)

            affine(0, 0, 0)
            make_z(0)
            affine(1, 0, 1)
            make_z(1)
            add_bo(0, 0, 0)

            def body(pair, half, par, first, last):
                if not last and not (isinstance(pair, int) and pair + 2 >= PAIRS):
                    affine(pair + 2, half + 1, par)
                gate(0, pair, par)
                gate(1, pair, par)
                if not first:
                    og_lo(1, pair - 1)
                og_lo(0, pair)
                if not last and not (isinstance(pair, int) and pair + 2 >= PAIRS):
                    make_z(pair + 2)
                if not last:
                    add_bo(pair + 1, half if par == 0 else half + 1, 1 - par)

            body(0, 0, 0, True, False)
            with pool.Fori(0, PAIRS // 2 - 2) as u:
                body(2 * u + 1, u, 1, False, False)
                body(2 * u + 2, u + 1, 0, False, False)
            body(PAIRS - 3, PAIRS // 2 - 2, 1, False, False)
            body(PAIRS - 2, PAIRS // 2 - 1, 0, False, False)
            body(PAIRS - 1, PAIRS // 2 - 1, 1, False, True)
            og_lo(1, PAIRS - 1)

        @block.scalar
        def _(act):
            def drain_hi(kind, number, dp, pair, par):
                psb = bank_of(kind, number)
                if kind == "o" or kind == "out":
                    return
                act.wait_ge(s_filled[kind] if kind != "ot" else s_drained["ot"], count(kind, number, pair))
                if kind == "zt":
                    nc.scalar.activation(zt[par][0][:, number, :], psb, ACT.Copy).then_inc(s_hi["zt"], 1)
                elif kind in "qk":
                    dst = (qt if kind == "q" else kt)[par][0]
                    nc.scalar.activation(dst[:, number, :], psb, ACT.Identity, bias=bias[kind][:, number:number + 1])\
                             .then_inc(s_hi[kind], 1)
                elif kind == "v":
                    nc.scalar.activation(vt[par][0][:, number, :, :, 0:HEAD_DIM],
                                         psb.rearrange("p (t h d) -> p t h d", t=NQ, h=NH), ACT.Copy)\
                             .then_inc(s_hi["v"], 1)
                elif kind == "g":
                    nc.scalar.activation(gt[:, par, number, :], psb, ACT.Tanh, bias=bias["g"][:, number:number + 1],
                                         scale=0.5).then_inc(s_drained["g"], 1)
                elif kind == "ot":
                    nc.scalar.activation(ogt[0][:, :, :], og[:, :, :], ACT.Copy).then_inc(s_hi["ot"], 1)

            def exps(chunk, c):
                act.wait_ge(s_max, chunk + 1)
                for n in range(4):
                    e = nc.scalar.activation(probs[:, c % 2, n, :], logits[c % 2][:, n // 2, (n % 2) * S:(n % 2 + 1) * S],
                                             ACT.Exp, bias=neg_max[:, c % 2, n:n + 1])
                e.then_inc(s_exp, 1)

            act.wait_ge(s_setup, 4)
            for kind, number in PROLOGUE:
                drain_hi(kind, number, 0, 0, 0)
            exps(0, 0)

            def body(pair, half, par, first, last):
                for c in range(CHUNKS):
                    chunk = CHUNKS * pair + c
                    for kind, number, dp in jobs(c, "A", first, last):
                        if kind != "ot":
                            drain_hi(kind, number, dp, pair + dp, (par + dp) % 2)
                    act.wait_ge(s_pt, chunk + 1)
                    nc.scalar.activation(pt[0][:, :, :, :].rearrange("p h n k -> p h (n k)"), pt_psum, ACT.Copy)\
                             .then_inc(s_pt_hi, 1)
                    for kind, number, dp in jobs(c, "A", first, last):
                        if kind == "ot":
                            drain_hi(kind, number, dp, pair + dp, (par + dp) % 2)
                    if c in EXPS_FIRST:
                        exps(chunk + 1, (c + 1) % CHUNKS)
                    for kind, number, dp in jobs(c, "B", first, last):
                        drain_hi(kind, number, dp, pair + dp, (par + dp) % 2)
                    if c not in EXPS_FIRST and not (last and c == CHUNKS - 1):
                        exps(chunk + 1, (c + 1) % CHUNKS)

            over_pairs(act, body)
            drain_hi("ot", 1, 0, PAIRS - 1, 1)

        @block.vector
        def _(dve):
            chain = [0]

            def link(ins):
                chain[0] += 1
                ins.then_inc(s_dve, 1)
                dve.wait_ge(s_dve, chain[0])

            dve.wait_ge(s_consts_loaded, 16 * 5)
            dve.wait_ge(s_weights_loaded, 16 * 5)
            lnw = lnw_row[:, :].unsqueeze(1).to_broadcast([P, NM, C])
            lnb = lnb_row[:, :].unsqueeze(1).to_broadcast([P, NM, C])
            for n in "qkvg":
                link(nc.vector.tensor_tensor(w_tmp[:, :, :], w_nat[n][:, :, :], lnb, ALU.mult))
                nc.vector.tensor_reduce(bias[n][:, :], w_tmp[:, :, :], X, ALU.add)
                link(nc.vector.tensor_tensor(w_nat[n][:, :, :], w_nat[n][:, :, :], lnw, ALU.mult))
            link(nc.vector.tensor_scalar(w_nat["q"][:, :, :], w_nat["q"][:, :, :], SCALE, None, ALU.mult))
            link(nc.vector.tensor_scalar(bias["q"][:, :], bias["q"][:, :], SCALE, None, ALU.mult))
            link(nc.vector.tensor_tensor(bias["g"][:, :], bias["g"][:, :], bg_col[:, :], ALU.add))
            link(nc.vector.tensor_scalar(bias["g"][:, :], bias["g"][:, :], 0.5, None, ALU.mult))
            link(nc.vector.tensor_reduce(v_scale[:, :], w_nat["v"][:, :, :], X, ALU.max, apply_absolute_value=True))
            link(nc.vector.tensor_scalar(v_scale[:, :], v_scale[:, :], TINY, None, ALU.max))
            link(nc.vector.reciprocal(v_rscale[:, :], v_scale[:, :]))
            link(nc.vector.tensor_tensor(bias["v"][:, :], bias["v"][:, :], v_rscale[:, :], ALU.mult))
            for m in range(NM):
                link(nc.vector.tensor_scalar(w_nat["v"][:, m, :], w_nat["v"][:, m, :], v_rscale[:, m:m + 1], None, ALU.mult))
            link(nc.vector.tensor_scalar(keep[:, :, :], mask_bias[:, :, :], 0.0, None, ALU.is_gt))
            link(nc.vector.tensor_reduce(kept_min[:, :], keep[:, :, :].rearrange("p q i -> p (q i)"), X, ALU.min))
            nc.vector.tensor_scalar(mask_bias[:, :, :], keep[:, :, :], -MASKED, MASKED, ALU.mult, ALU.add).then_inc(s_w_folded, 1)
            for n, name in enumerate("qkvgo"):
                dve.wait_ge(s_w_transposed, n + 1)
                ps = psum[:, n, :].rearrange("p (k n) -> p k n", k=NC)
                if name == "o":
                    for k in range(NC):
                        link(nc.vector.tensor_scalar(w_tmp[:, k, :], ps[:, k, :], v_scale[:, k:k + 1], None, ALU.mult))
                else:
                    link(nc.vector.tensor_copy(w_tmp[:, :, :], ps))
                link(nc.vector.tensor_copy(w_hi[name][:, :, :], w_tmp[:, :, :]))
                link(nc.vector.tensor_tensor(w_lo[name][:, :, :], w_tmp[:, :, :], w_hi[name][:, :, :].bitcast(F32), ALU.subtract))
            dve.wait_ge(s_w_transposed, 6)
            nc.vector.tensor_copy(mask_bias_t[0:MW, :, :], psum[0:MW, 5, 0:MT * S].rearrange("p (a s) -> p a s", a=MT)).then_inc(s_setup, 1)

            dve.wait_ge(s_w_transposed, 7)
            link(nc.vector.tensor_reduce(kept_row[0:1, 0:1], psum[0:1, 6, 0:P], X, ALU.min))
            nc.vector.tensor_scalar(masked_flag[0:1, 0:1], kept_row[0:1, 0:1], -1.0, 1.0, ALU.mult, ALU.add)\
                     .then_inc(s_setup, 1)

            def stat_tile(b, j, h):
                dve.wait_ge(s_stat_x[b], 16 * (h + 1))
                for g in range(GROUPS):
                    src = xs[:, b, :].rearrange("p (n c) -> p n c", c=C)[:, :, g * GC:(g + 1) * GC]
                    dst = gn_stats[:, g, bass.ds(j, 1), :].rearrange("p a s -> p (a s)")
                    last = nc.vector.bn_stats(dst, src)
                last.then_inc(s_stat_used, 1)

            with dve.Fori(0, STAT_TILES // 2) as h:
                stat_tile(0, 2 * h, h)
                stat_tile(1, 2 * h + 1, h)
            dve.wait_ge(s_stat_used, STAT_TILES)
            for g in range(GROUPS):
                last = nc.vector.bn_aggr(gn_part[:, g, :], gn_stats[:, g, :, :].rearrange("p j s -> p (j s)"))
            last.then_inc(s_gn_partial, 1)
            dve.wait_ge(s_gn_summed, 1)
            link(nc.vector.tensor_copy(gn_mean[:, :], psum[:, 6, 0:GROUPS]))
            link(nc.vector.tensor_tensor(gn_dev[:, :], gn_part[:, :, 0], gn_mean[:, :], ALU.subtract))
            link(nc.vector.tensor_tensor(gn_dev[:, :], gn_dev[:, :], gn_dev[:, :], ALU.mult))
            nc.vector.tensor_tensor(gn_dev[:, :], gn_dev[:, :], gn_part[:, :, 1], ALU.add).then_inc(s_gn_partial, 1)
            dve.wait_ge(s_gn_summed, 2)
            nc.vector.tensor_copy(gn_var[:, :], psum[:, 7, 0:GROUPS]).then_inc(s_gn_var, 1)
            dve.wait_ge(s_setup, 3)
            link(nc.vector.tensor_tensor(gn_shift[:, :], gn_mean[:, :], gn_rstd[:, :], ALU.mult))
            link(nc.vector.tensor_scalar(gn_shift[:, :], gn_shift[:, :], -1.0, None, ALU.mult))
            link(nc.vector.tensor_copy(gn_scale_row[:, :].rearrange("p (g c) -> p g c", c=GC),
                                       gn_rstd[:, :].unsqueeze(2).to_broadcast([P, GROUPS, GC])))
            link(nc.vector.tensor_copy(gn_shift_row[:, :].rearrange("p (g c) -> p g c", c=GC),
                                       gn_shift[:, :].unsqueeze(2).to_broadcast([P, GROUPS, GC])))
            nc.vector.memset(row_rstd[:, 0:1], 0.0).then_inc(s_gn_rows, 1)
            nc.vector.memset(row_mv[:, 0, 0:1], 0.0).then_inc(s_setup, 1)

            def row_statistics(pair):
                dve.wait_ge(s_affine, 2 * pair + 2)
                for r in range(NQ * 2):
                    last = nc.vector.bn_stats(row_stats[:, r, :], xn[:, r, :])
                last.then_inc(s_row_stats_own, 1)

            def row_aggregate(pair):
                dve.wait_ge(s_row_stats_own, pair + 1)
                nc.vector.memset(wait_carrier[:, :], 0.0)
                for r in range(NQ * 2):
                    last = nc.vector.bn_aggr(row_mv[:, r, :], row_stats[:, r, :])
                last.then_inc(s_row_stats, 1)

            def maxes(chunk, c):
                dve.wait_ge(s_logits, chunk + 1)
                nc.vector.tensor_reduce(neg_max[:, c % 2, :], logits[c % 2].rearrange("p h (q k) -> p (h q) k", q=NQ),
                                        X, ALU.max, negate=True).then_inc(s_max, 1)

            def drain(kind, number, pair, par):
                psb = bank_of(kind, number)
                if kind in ("zt", "q", "k", "v"):
                    dve.wait_ge(s_hi[kind], count(kind, number, pair))
                if kind == "zt":
                    hi, lo = zt[par]
                    nc.vector.tensor_tensor(lo[:, number, :], psb, hi[:, number, :].bitcast(F32), ALU.subtract)\
                             .then_inc(s_drained["zt"], 1)
                elif kind in ("q", "k"):
                    hi, lo = (qt if kind == "q" else kt)[par]
                    nc.vector.scalar_tensor_tensor(lo[:, number, :], psb, bias[kind][:, number:number + 1],
                                                   hi[:, number, :].bitcast(F32), ALU.add, ALU.subtract)\
                             .then_inc(s_drained[kind], 1)
                elif kind == "v":
                    hi, lo = vt[par]
                    nc.vector.tensor_tensor(lo[:, number, :, :, 0:HEAD_DIM],
                                            psb.rearrange("p (t h d) -> p t h d", t=NQ, h=NH),
                                            hi[:, number, :, :, 0:HEAD_DIM], ALU.subtract)\
                             .then_inc(s_drained["v"], 1)
                elif kind == "ot":
                    dve.wait_ge(s_filled["ot"], count("ot", number, pair))
                    dve.wait_ge(s_gate, 4 * pair + 4)
                    for m in range(NM):
                        last = nc.vector.scalar_tensor_tensor(og[:, m, :], psb[:, m * S:(m + 1) * S], bias["v"][:, m:m + 1],
                                                              gt[:, par, m, number * S:(number + 1) * S],
                                                              ALU.add, ALU.mult)
                    last.then_inc(s_drained["ot"], 1)
                elif kind == "out":
                    dve.wait_ge(s_filled["out"], count("out", number, pair))
                    dve.wait_ge(s_xb, pair + 1)
                    for q in range(NQ):
                        dst = xb[:, par, q, number, :]
                        mask_col = keep[:, q, bass.ds(2 * pair + number, 1)]
                        last = nc.vector.scalar_tensor_tensor(dst, psb[:, q * C:(q + 1) * C], mask_col, dst,
                                                              ALU.mult, ALU.add)
                    last.then_inc(s_drained["out"], 1)

            def normalise(chunk, c):
                dve.wait_ge(s_filled["o"], chunk + 1)
                column, hp = c // 4, c % 4
                o = bank_of("o", c)[:, 0:4 * (HEAD_DIM + 1)].rearrange("p (h q d) -> p h q d", h=2, q=NQ)
                nc.vector.reciprocal(row_rsum[:, :].rearrange("p (h q) -> p h q", h=2), o[:, :, :, HEAD_DIM])\
                         .then_inc(s_rsum, 1)
                dve.wait_ge(s_rsum, chunk + 1)
                by = row_rsum[:, :].rearrange("p (h q) -> p h q", h=2).unsqueeze(3).to_broadcast([P, 2, NQ, HEAD_DIM])
                dst = o_rows[:, column, :, 2 * hp * HEAD_DIM:2 * (hp + 1) * HEAD_DIM].rearrange("p q (h d) -> p h q d", h=2)
                nc.vector.tensor_tensor(dst, o[:, :, :, 0:HEAD_DIM], by, ALU.mult).then_inc(s_drained["o"], 1)

            for pair in range(2):
                row_statistics(pair)
                row_aggregate(pair)
            for kind, number in PROLOGUE:
                drain(kind, number, 0, 0)
            maxes(0, 0)

            def body(pair, half, par, first, last):
                for c in range(CHUNKS):
                    chunk = CHUNKS * pair + c
                    if not (last and c == CHUNKS - 1):
                        maxes(chunk + 1, (c + 1) % CHUNKS)
                    for kind, number, dp in jobs(c, "A", first, last):
                        drain(kind, number, pair + dp, (par + dp) % 2)
                    if not (first and c == 0):
                        normalise(chunk - 1, (c - 1) % CHUNKS)
                    if not last and not (isinstance(pair, int) and pair + 2 >= PAIRS):
                        if c == 2:
                            row_statistics(pair + 2)
                        if c == 3:
                            row_aggregate(pair + 2)
                    dve.wait_ge(s_pt_hi, chunk + 1)
                    nc.vector.tensor_tensor(pt[1][:, :, :, :].rearrange("p h n k -> p h (n k)"), pt_psum,
                                            pt[0][:, :, :, :].rearrange("p h n k -> p h (n k)"), ALU.subtract)\
                             .then_inc(s_pt_lo, 1)
                    for kind, number, dp in jobs(c, "B", first, last):
                        drain(kind, number, pair + dp, (par + dp) % 2)

            body(0, 0, 0, True, False)
            with dve.Fori(0, PAIRS // 2 - 2) as u:
                body(2 * u + 1, u, 1, False, False)
                body(2 * u + 2, u + 1, 0, False, False)
            body(PAIRS - 3, PAIRS // 2 - 2, 1, False, False)
            body(PAIRS - 2, PAIRS // 2 - 1, 0, False, False)
            body(PAIRS - 1, PAIRS // 2 - 1, 1, False, True)
            normalise(CHUNKS * PAIRS - 1, CHUNKS - 1)
            drain("ot", 1, PAIRS - 1, 1)
            drain("out", 1, PAIRS - 1, 1)

        @block.tensor
        def _(pe):
            pe.wait_ge(s_const, 1)
            pe.wait_ge(s_w_folded, 1)
            for n, name in enumerate("qkvgo"):
                for k in range(NC):
                    for m in range(NM):
                        last = nc.tensor.transpose(psum[:, n, k * HD + m * P:k * HD + (m + 1) * P],
                                                   w_nat[name][:, m, k * P:(k + 1) * P], ident[:, :])
                last.then_inc(s_w_transposed, 1)
            for a in range(MT):
                for q in range(NQ):
                    last = nc.tensor.transpose(psum[0:MW, 5, a * S + q * P:a * S + (q + 1) * P],
                                               mask_bias[:, q, a * MW:(a + 1) * MW], ident[:, :])
            last.then_inc(s_w_transposed, 1)
            nc.tensor.transpose(psum[0:1, 6, 0:P], kept_min[:, 0:1], ident[:, :]).then_inc(s_w_transposed, 1)
            pe.wait_ge(s_gn_partial, 1)
            nc.tensor.matmul(psum[:, 6, 0:GROUPS], mean_mat[:, :], gn_part[:, :, 0], start=True, stop=True)\
                     .then_inc(s_gn_summed, 1)
            pe.wait_ge(s_gn_partial, 2)
            nc.tensor.matmul(psum[:, 7, 0:GROUPS], mean_mat[:, :], gn_dev[:, :], start=True, stop=True)\
                     .then_inc(s_gn_summed, 1)
            PASSES = ((0, 0), (0, 1), (1, 0))
            use_mask = [False]
            held = {}

            def run_job(kind, number, dp, pair, par):
                bank = BANK[kind, number]
                if bank in held:
                    k0, n0, d0 = held[bank]
                    pe.wait_ge(s_drained[k0], count(k0, n0, pair + d0))
                held[bank] = (kind, number, dp)
                ps = job_psum[bank]
                at = pair + dp
                if kind == "zt":
                    pe.wait_ge(s_z, 2 * at + 2)
                    for i in range(2):
                        for q in range(NQ):
                            last = nc.tensor.transpose(ps[:, i * S + q * P:i * S + (q + 1) * P],
                                                       z[:, q, i, number * P:(number + 1) * P], ident[:, :])
                elif kind in ("q", "k", "g"):
                    pe.wait_ge(s_drained["zt"], 2 * at + 2)
                    n = 0
                    for c in range(NC):
                        for a, b in PASSES:
                            w = (w_hi, w_lo)[a][kind]
                            last = nc.tensor.matmul(ps, w[:, c, number * P:(number + 1) * P], zt[par][b][:, c, :],
                                                    start=(n == 0), stop=(n == 5))
                            n += 1
                elif kind == "v":
                    for q in range(NQ):
                        n = 0
                        for c in range(NC):
                            for a, b in PASSES:
                                w = (w_hi, w_lo)[b]["v"]
                                lhs = zt[par][a][:, c, number * S + q * P:number * S + (q + 1) * P]
                                last = nc.tensor.matmul(ps[:, q * HD:(q + 1) * HD], lhs, w[:, c, :],
                                                        start=(n == 0), stop=(n == 5))
                                n += 1
                elif kind == "ot":
                    pe.wait_ge(s_drained["o"], 8 * at + 4 * (number + 1))
                    for m in range(NM):
                        for q in range(NQ):
                            last = nc.tensor.transpose(ps[:, m * S + q * P:m * S + (q + 1) * P],
                                                       o_rows[:, number, q, m * P:(m + 1) * P], ident[:, :])
                elif kind == "out":
                    pe.wait_ge(s_og_lo, count("ot", number, at))
                    for q in range(NQ):
                        n = 0
                        for m in range(NM):
                            for a, b in PASSES:
                                w = (w_hi, w_lo)[b]["o"]
                                last = nc.tensor.matmul(ps[:, q * C:(q + 1) * C], ogt[a][:, m, q * P:(q + 1) * P],
                                                        w[:, m, :], start=(n == 0), stop=(n == 5))
                                n += 1
                last.then_inc(s_filled[kind], 1)

            def run_logits(chunk, c, pair, par):
                if not (isinstance(chunk, int) and chunk < 2):
                    pe.wait_ge(s_exp, chunk - 1)
                pe.wait_ge(s_drained["q"], 2 * pair + (c % 4) // 2 + 1)
                pe.wait_ge(s_drained["k"], 2 * pair + (c % 4) // 2 + 1)
                column, hp = c // 4, c % 4
                m = hp // 2
                masked = use_mask[0]
                if masked:
                    for h in range(2):
                        for a in range(MT):
                            hot = column_hot[0:MW, bass.ds(a * I + 2 * pair + column, 1)].to_broadcast([MW, P])
                            src = mask_bias_t[0:MW, a:a + 1, :].to_broadcast([MW, NQ, S])
                            nc.tensor.matmul(logits[c % 2][:, h, :].rearrange("p (q k) -> p q k", q=NQ), hot, src,
                                             start=(a == 0), stop=False, skip_group_check=True)
                for q in range(NQ):
                    for n, (a, b) in enumerate(PASSES):
                        for h in range(2):
                            rows = slice((2 * hp + h) % 4 * HEAD_DIM, ((2 * hp + h) % 4 + 1) * HEAD_DIM)
                            last = nc.tensor.matmul(logits[c % 2][:, h, q * S:(q + 1) * S],
                                                    qt[par][a][rows, m, column * S + q * P:column * S + (q + 1) * P],
                                                    kt[par][b][rows, m, column * S:(column + 1) * S],
                                                    start=(n == 0 and not masked), stop=(n == 2), skip_group_check=True)
                last.then_inc(s_logits, 1)

            def run_weighted_sum(chunk, c, par, pair, dp):
                bank = BANK["o", c]
                k0, n0, d0 = held[bank]
                pe.wait_ge(s_drained[k0], count(k0, n0, pair + d0))
                held[bank] = ("o", c, dp)
                pe.wait_ge(s_pt_lo, chunk + 1)
                pe.wait_ge(s_drained["v"], 2 * (pair + dp) + c // 4 + 1)
                column, hp = c // 4, c % 4
                for h in range(2):
                    for q in range(NQ):
                        n = 0
                        for k in range(NQ):
                            for a, b in PASSES:
                                o = (h * NQ + q) * (HEAD_DIM + 1)
                                w = HEAD_DIM + (b == 0)
                                last = nc.tensor.matmul(job_psum[bank][:, o:o + w], pt[a][:, h, k * NQ + q, :],
                                                        vt[par][b][:, column, k, 2 * hp + h, 0:w],
                                                        start=(n == 0), stop=(n == 5))
                                n += 1
                last.then_inc(s_filled["o"], 1)

            def run_transposes(chunk, c):
                pe.wait_ge(s_exp, chunk + 1)
                if not (isinstance(chunk, int) and chunk < 1):
                    pe.wait_ge(s_pt_lo, chunk)
                for h in range(2):
                    for k in range(NQ):
                        for q in range(NQ):
                            n = k * NQ + q
                            last = nc.tensor.transpose(pt_psum[:, h, n * P:(n + 1) * P],
                                                       probs[:, c % 2, h * NQ + q, k * P:(k + 1) * P], ident[:, :])
                last.then_inc(s_pt, 1)

            def body(pair, half, par, first, last):
                for c in range(CHUNKS):
                    chunk = CHUNKS * pair + c
                    if c < CHUNKS - 1:
                        run_logits(chunk + 1, c + 1, pair, par)
                    elif not last:
                        run_logits(chunk + 1, 0, pair + 1, 1 - par)
                    for kind, number, dp in jobs(c, "A", first, last):
                        run_job(kind, number, dp, pair, (par + dp) % 2)
                    if c > 0:
                        run_weighted_sum(chunk - 1, c - 1, par, pair, 0)
                    elif not first:
                        run_weighted_sum(chunk - 1, CHUNKS - 1, 1 - par, pair, -1)
                    run_transposes(chunk, c)
                    for kind, number, dp in jobs(c, "B", first, last):
                        run_job(kind, number, dp, pair, (par + dp) % 2)
                for b, (k0, n0, d0) in list(held.items()):
                    held[b] = (k0, n0, d0 - 1)

            def attention():
                held.clear()
                for kind, number in PROLOGUE:
                    run_job(kind, number, 0, 0, 0)
                run_logits(0, 0, 0, 0)
                over_pairs(pe, body)
                run_weighted_sum(CHUNKS * PAIRS - 1, CHUNKS - 1, 1, PAIRS, -1)
                run_job("ot", 1, -1, PAIRS, 1)
                run_job("out", 1, -1, PAIRS, 1)

            pe.wait_ge(s_setup, 4)
            masked_rows = pe.value_load(masked_flag[0:1, 0:1], min_val=0, max_val=1)
            with pe.If(masked_rows > 0):
                use_mask[0] = True
                attention()
            with pe.Else():
                use_mask[0] = False
                attention()


_INS = ["x", "L0_conv_msa_mask", "L0_conv_ln_w", "L0_conv_ln_b", "L0_conv_wq", "L0_conv_wk", "L0_conv_wv",
        "L0_conv_wg", "L0_conv_bg", "L0_conv_wo", "L0_conv_bo"]


def kernel(**inputs):
    import numpy as _np
    import concourse.bacc as _bacc
    from concourse import mybir as _mybir
    from concourse.bass_utils import run_bass_kernel_spmd as _run

    nc = _bacc.Bacc("TRN2", target_bir_lowering=False, num_devices=1)
    arrays, args = {}, []
    for name in _INS:
        a = _np.ascontiguousarray(inputs[name])
        arrays[f"in_{name}_dram"] = a
        args.append(nc.dram_tensor(f"in_{name}_dram", a.shape, _mybir.dt.from_np(a.dtype), kind="ExternalInput").ap())
    shape = arrays["in_x_dram"].shape
    args.append(nc.dram_tensor("out_0_dram", shape, _mybir.dt.float32, kind="ExternalOutput").ap())
    build_msa(nc, *args)
    r = _run(nc, [arrays], core_ids=[0])
    return r.results[0]["out_0_dram"]
```
